# Optimizing a Trainium2 kernel written in Bass

```python
import numpy as np
import jax
import jax.numpy as jnp

def _softmax(x, axis=-1):
    return jax.nn.softmax(x, axis=axis)

def _gelu(x):
    return jax.nn.gelu(x, approximate=True)

def _silu(x):
    return jax.nn.silu(x)

def _sigmoid(x):
    return jax.nn.sigmoid(x)

def _layernorm(x, axis=-1, eps=1e-05):
    m = jnp.mean(x, axis=axis, keepdims=True)
    v = jnp.var(x, axis=axis, keepdims=True)
    return (x - m) / jnp.sqrt(v + eps)

def _scatter_add(tgt, idx, src, axis=0):
    return tgt.at[idx].add(src)

def _segment_sum(src, seg, n):
    return jax.ops.segment_sum(src, seg, n)
kernel_name = 'mk_dlrm_tower_d1_rec_r8_ac9934'

def setup_inputs(seed: int=0):
    np.random.seed(seed)
    _w = jnp.asarray

    def _rec_inputs():
        import jax
        import jax.numpy as jnp
        _tk = jax.random.key(seed)
        ids = jnp.stack([jax.random.randint(jax.random.fold_in(_tk, 200 + f), (512,), 0, v, jnp.int32) for f, v in enumerate([125000, 1000, 1000, 1250, 1000, 12500, 12500, 1250, 12500, 1000, 1000, 12500, 12500, 1000, 1000, 12500, 1000, 1000, 12500, 1250, 12500, 1250, 12500, 1000, 1000, 1000])], axis=1)
        tbl_0 = 0.05 * jax.random.normal(jax.random.fold_in(_tk, 500 + 0), (125000, 128), jnp.float32)
        tbl_1 = 0.05 * jax.random.normal(jax.random.fold_in(_tk, 500 + 1), (1000, 128), jnp.float32)
        tbl_2 = 0.05 * jax.random.normal(jax.random.fold_in(_tk, 500 + 2), (1000, 128), jnp.float32)
        tbl_3 = 0.05 * jax.random.normal(jax.random.fold_in(_tk, 500 + 3), (1250, 128), jnp.float32)
        tbl_4 = 0.05 * jax.random.normal(jax.random.fold_in(_tk, 500 + 4), (1000, 128), jnp.float32)
        tbl_5 = 0.05 * jax.random.normal(jax.random.fold_in(_tk, 500 + 5), (12500, 128), jnp.float32)
        tbl_6 = 0.05 * jax.random.normal(jax.random.fold_in(_tk, 500 + 6), (12500, 128), jnp.float32)
        tbl_7 = 0.05 * jax.random.normal(jax.random.fold_in(_tk, 500 + 7), (1250, 128), jnp.float32)
        tbl_8 = 0.05 * jax.random.normal(jax.random.fold_in(_tk, 500 + 8), (12500, 128), jnp.float32)
        tbl_9 = 0.05 * jax.random.normal(jax.random.fold_in(_tk, 500 + 9), (1000, 128), jnp.float32)
        tbl_10 = 0.05 * jax.random.normal(jax.random.fold_in(_tk, 500 + 10), (1000, 128), jnp.float32)
        tbl_11 = 0.05 * jax.random.normal(jax.random.fold_in(_tk, 500 + 11), (12500, 128), jnp.float32)
        tbl_12 = 0.05 * jax.random.normal(jax.random.fold_in(_tk, 500 + 12), (12500, 128), jnp.float32)
        tbl_13 = 0.05 * jax.random.normal(jax.random.fold_in(_tk, 500 + 13), (1000, 128), jnp.float32)
        tbl_14 = 0.05 * jax.random.normal(jax.random.fold_in(_tk, 500 + 14), (1000, 128), jnp.float32)
        tbl_15 = 0.05 * jax.random.normal(jax.random.fold_in(_tk, 500 + 15), (12500, 128), jnp.float32)
        tbl_16 = 0.05 * jax.random.normal(jax.random.fold_in(_tk, 500 + 16), (1000, 128), jnp.float32)
        tbl_17 = 0.05 * jax.random.normal(jax.random.fold_in(_tk, 500 + 17), (1000, 128), jnp.float32)
        tbl_18 = 0.05 * jax.random.normal(jax.random.fold_in(_tk, 500 + 18), (12500, 128), jnp.float32)
        tbl_19 = 0.05 * jax.random.normal(jax.random.fold_in(_tk, 500 + 19), (1250, 128), jnp.float32)
        tbl_20 = 0.05 * jax.random.normal(jax.random.fold_in(_tk, 500 + 20), (12500, 128), jnp.float32)
        tbl_21 = 0.05 * jax.random.normal(jax.random.fold_in(_tk, 500 + 21), (1250, 128), jnp.float32)
        tbl_22 = 0.05 * jax.random.normal(jax.random.fold_in(_tk, 500 + 22), (12500, 128), jnp.float32)
        tbl_23 = 0.05 * jax.random.normal(jax.random.fold_in(_tk, 500 + 23), (1000, 128), jnp.float32)
        tbl_24 = 0.05 * jax.random.normal(jax.random.fold_in(_tk, 500 + 24), (1000, 128), jnp.float32)
        tbl_25 = 0.05 * jax.random.normal(jax.random.fold_in(_tk, 500 + 25), (1000, 128), jnp.float32)
        _rk = jax.random.fold_in(_tk, 7)
        r_dense_features = -0.000520686 + 1.00062 * jax.random.normal(jax.random.fold_in(_rk, 101), (512, 128), jnp.float32)
        W_top1 = 0.0405887 * jax.random.normal(jax.random.fold_in(_tk, 801), (607, 512), jnp.float32)
        W_top2 = 0.0441942 * jax.random.normal(jax.random.fold_in(_tk, 802), (512, 256), jnp.float32)
        W_top3 = 0.0625 * jax.random.normal(jax.random.fold_in(_tk, 803), (256, 1), jnp.float32)
        b_top1 = jnp.zeros((512,), jnp.float32)
        b_top2 = jnp.zeros((256,), jnp.float32)
        return (r_dense_features, ids, tbl_0, tbl_1, tbl_2, tbl_3, tbl_4, tbl_5, tbl_6, tbl_7, tbl_8, tbl_9, tbl_10, tbl_11, tbl_12, tbl_13, tbl_14, tbl_15, tbl_16, tbl_17, tbl_18, tbl_19, tbl_20, tbl_21, tbl_22, tbl_23, tbl_24, tbl_25, W_top1, b_top1, W_top2, b_top2, W_top3)
    r_dense_features, ids, tbl_0, tbl_1, tbl_2, tbl_3, tbl_4, tbl_5, tbl_6, tbl_7, tbl_8, tbl_9, tbl_10, tbl_11, tbl_12, tbl_13, tbl_14, tbl_15, tbl_16, tbl_17, tbl_18, tbl_19, tbl_20, tbl_21, tbl_22, tbl_23, tbl_24, tbl_25, W_top1, b_top1, W_top2, b_top2, W_top3 = _rec_inputs()

    def _L0_rec_setup():
        import jax, jax.numpy as jnp
        import numpy as np
        F = 26
        key = jax.random.key(seed)
        k1, k2 = jax.random.split(key)
        B, D = (2048, 128)
        dense_features = jax.random.normal(k1, (B, D), dtype=jnp.float32)
        sparse_features = jax.random.normal(k2, (B, F, D), dtype=jnp.float32)
        return {'dense_features': dense_features, 'sparse_features': sparse_features}
    _L0_rec_all = _L0_rec_setup()
    _L0_rec_in = {k: v for k, v in _L0_rec_all.items() if k in ()}
    del _L0_rec_all
    return {'r_dense_features': r_dense_features, 'ids': ids, 'tbl_0': tbl_0, 'tbl_1': tbl_1, 'tbl_2': tbl_2, 'tbl_3': tbl_3, 'tbl_4': tbl_4, 'tbl_5': tbl_5, 'tbl_6': tbl_6, 'tbl_7': tbl_7, 'tbl_8': tbl_8, 'tbl_9': tbl_9, 'tbl_10': tbl_10, 'tbl_11': tbl_11, 'tbl_12': tbl_12, 'tbl_13': tbl_13, 'tbl_14': tbl_14, 'tbl_15': tbl_15, 'tbl_16': tbl_16, 'tbl_17': tbl_17, 'tbl_18': tbl_18, 'tbl_19': tbl_19, 'tbl_20': tbl_20, 'tbl_21': tbl_21, 'tbl_22': tbl_22, 'tbl_23': tbl_23, 'tbl_24': tbl_24, 'tbl_25': tbl_25, 'W_top1': W_top1, 'b_top1': b_top1, 'W_top2': W_top2, 'b_top2': b_top2, 'W_top3': W_top3}

def reference(r_dense_features, ids, tbl_0, tbl_1, tbl_2, tbl_3, tbl_4, tbl_5, tbl_6, tbl_7, tbl_8, tbl_9, tbl_10, tbl_11, tbl_12, tbl_13, tbl_14, tbl_15, tbl_16, tbl_17, tbl_18, tbl_19, tbl_20, tbl_21, tbl_22, tbl_23, tbl_24, tbl_25, W_top1, b_top1, W_top2, b_top2, W_top3):
    import jax
    import jax.numpy as jnp

    def _L0_rec_ref(dense_features, sparse_features):
        import jax, jax.numpy as jnp
        import numpy as np
        F = 26
        B, D = dense_features.shape
        combined = jnp.concatenate((dense_features[:, None, :], sparse_features), axis=1)
        interactions = jnp.einsum('bfd,bgd->bfg', combined, combined)
        iu, ju = jnp.triu_indices(F + 1, k=1)
        interactions_flat = interactions[:, iu, ju]
        return jnp.concatenate((dense_features, interactions_flat), axis=1)
    e = jnp.stack([tbl_0[ids[:, 0]], tbl_1[ids[:, 1]], tbl_2[ids[:, 2]], tbl_3[ids[:, 3]], tbl_4[ids[:, 4]], tbl_5[ids[:, 5]], tbl_6[ids[:, 6]], tbl_7[ids[:, 7]], tbl_8[ids[:, 8]], tbl_9[ids[:, 9]], tbl_10[ids[:, 10]], tbl_11[ids[:, 11]], tbl_12[ids[:, 12]], tbl_13[ids[:, 13]], tbl_14[ids[:, 14]], tbl_15[ids[:, 15]], tbl_16[ids[:, 16]], tbl_17[ids[:, 17]], tbl_18[ids[:, 18]], tbl_19[ids[:, 19]], tbl_20[ids[:, 20]], tbl_21[ids[:, 21]], tbl_22[ids[:, 22]], tbl_23[ids[:, 23]], tbl_24[ids[:, 24]], tbl_25[ids[:, 25]]], axis=1)
    z = _L0_rec_ref(r_dense_features, e)
    z = z.reshape(z.shape[0], -1)
    h = jnp.concatenate([z, r_dense_features], axis=1)
    h = jnp.maximum(h @ W_top1 + b_top1, 0.0)
    h = jnp.maximum(h @ W_top2 + b_top2, 0.0)
    y = h @ W_top3
    return y

_drawn_inputs = setup_inputs


def setup_inputs(seed=0):
    import zlib

    import numpy as np

    out = dict(_drawn_inputs(seed))
    spreads = {'b_top1': (0.0, 0.1), 'b_top2': (0.0, 0.1)}
    factors = {}
    for name, (base, spread) in spreads.items():
        noise = np.random.default_rng([zlib.crc32(name.encode()), seed]).standard_normal(out[name].shape)
        drawn = base * np.exp(spread * noise) if base else spread * noise
        out[name] = jnp.asarray(drawn.astype(out[name].dtype))
    for name, factor in factors.items():
        out[name] = (out[name] * factor).astype(out[name].dtype)
    return out
```

```python
from contextlib import ExitStack

import concourse.bass as bass
from concourse import mybir

F32 = mybir.dt.float32
I32 = mybir.dt.int32
ALU = mybir.AluOpType
ACT = mybir.ActivationFunctionType

P = 128
Q = 32
GROUP = 4
PACK = 4
CHUNK = 8


def dlrm_tower(nc, dense, ids, tables, w1, b1, w2, b2, w3, out):
    B, D = dense.shape
    NT = len(tables)
    F = NT + 1
    T = B // P
    N1, N2 = w2.shape
    M1, M2 = N1 // P, N2 // P
    PAIRS = F * (F - 1) // 2
    GROUPS = -(-F // GROUP)
    ZC = -(-(F - 1) // 4)
    CHUNKS = P // (PACK * CHUNK)
    assert M1 == 4 and M2 == 2 and D == P and B == T * P and F <= Q and w1.shape[0] == 2 * D + PAIRS

    def quads(c):
        return min(4, F - 1 - 4 * c)

    ctx = ExitStack()
    with ctx:
        def sb(name, shape, dt=F32):
            return ctx.enter_context(nc.sbuf_tensor(name, shape, dt))

        def ps(name, shape):
            return ctx.enter_context(nc.psum_tensor(name, shape, F32))

        def sem(name):
            return ctx.enter_context(nc.semaphore(name))

        ids_sb = sb("ids_sb", [P, T, NT], I32)
        rows = sb("rows", [P, T, F, D])
        ident = sb("ident", [P, P])
        xT = sb("xT", [P, T, P, Q])
        z = sb("z", [P, ZC, B])
        w_pair = sb("w_pair", [P, ZC, N1])
        w_dense = sb("w_dense", [P, N1])
        w_dense2 = sb("w_dense2", [P, N1])
        w2_sb = sb("w2_sb", [P, M1, N2])
        w3_sb = sb("w3_sb", [P, M2])
        b1_sb = sb("b1_sb", [P, M1])
        b2_sb = sb("b2_sb", [P, M2])
        h1 = sb("h1", [P, M1, B])
        h2 = sb("h2", [P, M2, B])
        y = sb("y", [1, P, T])

        turned = [ps(f"turned{i}", [P, GROUP, P]) for i in range(2)]
        gram = [ps(f"gram{i}", [P, CHUNK, P]) for i in range(2)]
        mlp = [ps(f"mlp{e}", [P, 4, P]) for e in range(2)]
        H1 = M1 // 2
        p1 = [mlp[m // H1][:, m % H1, :] for m in range(M1)]
        p2 = [mlp[m][:, H1, :] for m in range(M2)]
        p3 = mlp[0][0:1, H1 + 1, :]

        ids_in = sem("ids_in")
        dense_in = sem("dense_in")
        small_in = sem("small_in")
        wd_in = sem("wd_in")
        pair_in = sem("pair_in")
        gathered = [[sem(f"gathered{t}_{k}") for k in range(GROUPS)] for t in range(T)]
        ident_zero = sem("ident_zero")
        ident_ready = sem("ident_ready")
        pair_zero = sem("pair_zero")
        pads_zero = sem("pads_zero")
        wd_ready = sem("wd_ready")
        turned_ready = sem("turned_ready")
        xt_act = sem("xt_act")
        xt_dve = sem("xt_dve")
        gram_ready = sem("gram_ready")
        z_act = sem("z_act")
        z_dve = sem("z_dve")
        p1_ready = sem("p1_ready")
        h1_act = sem("h1_act")
        h1_dve = sem("h1_dve")
        p2_ready = sem("p2_ready")
        h2_act = sem("h2_act")
        h2_dve = sem("h2_dve")
        p3_ready = sem("p3_ready")
        y_ready = sem("y_ready")
        out_done = sem("out_done")
        block = ctx.enter_context(nc.Block())

        dense_at = [0, D + PAIRS]

        def pair_loads():
            for f in range(F - 1):
                c, j = divmod(f, 4)
                if j:
                    if quads(c) > j:
                        yield f, j, quads(c) - j, c, 1
                    c += 1
                full = sum(1 for k in range(c, ZC) if quads(k) == 4)
                if full:
                    yield f, 0, 4, c, full
                if c + full < ZC:
                    yield f, 0, quads(c + full), c + full, 1

        n_pair = len(list(pair_loads()))

        @block.sync
        def _(sp):
            sp.dma_start(ids_sb[:, :, :], ids.rearrange("(p t) f -> p t f", t=T)).then_inc(ids_in, 16)
            sp.dma_start(rows[:, :, 0, :], dense.rearrange("(p t) d -> p t d", t=T)).then_inc(dense_in, 16)
            sp.dma_start(w_dense[:, :], w1[0:D, :]).then_inc(wd_in, 16)
            sp.dma_start(w_dense2[:, :], w1[D + PAIRS:2 * D + PAIRS, :]).then_inc(wd_in, 16)
            sp.dma_start(b1_sb[:, :], b1.rearrange("(p m) -> p m", m=M1)).then_inc(small_in, 16)
            sp.dma_start(b2_sb[:, :], b2.rearrange("(p m) -> p m", m=M2)).then_inc(small_in, 16)
            sp.dma_start(w3_sb[:, :], w3.rearrange("(p m) o -> p (m o)", m=M2)).then_inc(small_in, 16)
            sp.dma_start(w2_sb[:, :, :], w2.rearrange("(p m) n -> p m n", m=M1)).then_inc(small_in, 16)
            sp.wait_ge(pair_zero, 1)
            for f, j, nj, c, n in pair_loads():
                pair = D + f * F - f * (f + 1) // 2 - f - 1
                first = pair + 4 * c + j + 1
                src = w1[first:first + 1, :]
                src = bass.AP(src.tensor, src.offset, [[N1, nj], [4 * N1, n], [1, N1]])
                sp.dma_start(w_pair[Q * j + f:Q * (j + nj - 1) + f + 1:Q, c:c + n, :], src).then_inc(pair_in, 16)
            sp.wait_ge(y_ready, T)
            sp.dma_start(out.rearrange("b o -> o b"), y[:, :, :].rearrange("o p t -> o (p t)")).then_inc(out_done, 16)
            sp.wait_ge(out_done, 16)

        @block.gpsimd
        def _(pool):
            pool.memset(ident[:, :], 0.0).then_inc(ident_zero, 1)
            pool.wait_ge(ident_zero, 1)
            pool.affine_select(out=ident[:, :], in_=ident[:, :], compare_op=ALU.not_equal, fill=1.0,
                               base=0, pattern=[[-1, P]], channel_multiplier=1).then_inc(ident_ready, 1)
            pool.wait_ge(ids_in, 16)
            for t in range(T):
                for f in range(1, F):
                    pool.indirect_dma_start(
                        rows[:, t, f, :], None, tables[f - 1],
                        bass.IndirectOffsetOnAxis(ap=ids_sb[:, t, f - 1:f], axis=0),
                    ).then_inc(gathered[t][f // GROUP], 16)

        def group(k):
            return range(GROUP * k, min(GROUP * (k + 1), F))

        def collect(eng, copy, t, k, done):
            i = t * GROUPS + k
            n = len(group(k))
            eng.wait_ge(turned_ready, i + 1)
            copy(xT[:, t, :, GROUP * k:GROUP * k + n], turned[i % 2][:, 0:n, :].rearrange("p f b -> p b f")).then_inc(done, 1)

        def regroup(eng, copy, t, m, samples, done):
            n = t * CHUNKS + m
            eng.wait_ge(gram_ready, n + 1)
            for s in samples:
                for j in range(4):
                    nc_j = sum(1 for c in range(ZC) if quads(c) > j)
                    g0 = F * s + j + 1
                    src = gram[n % 2][Q * s:Q * (s + 1), :, g0:g0 + 4 * (nc_j - 1) + 1:4]
                    at = t * P + PACK * CHUNK * m + s
                    dst = z[Q * j:Q * (j + 1), 0:nc_j, at:at + PACK * (CHUNK - 1) + 1:PACK]
                    last = copy(dst, src.rearrange("p q c -> p c q"))
            last.then_inc(done, 1)

        @block.scalar
        def _(act):
            def copy(dst, src):
                return nc.scalar.activation(dst, src, ACT.Copy)

            for t in range(T):
                at = slice(t * P, (t + 1) * P)
                for k in range(GROUPS):
                    if (t * GROUPS + k) % 2 == 0:
                        collect(act, copy, t, k, xt_act)
                for m in range(CHUNKS):
                    regroup(act, copy, t, m, (2, 3), z_act)
                if t == 0:
                    act.wait_ge(small_in, 64)
                act.wait_ge(p1_ready, t + 1)
                for m in range(H1, M1):
                    last = nc.scalar.activation(h1[:, m, at], p1[m], ACT.Relu, bias=b1_sb[:, m:m + 1])
                last.then_inc(h1_act, 1)
                act.wait_ge(p2_ready, t + 1)
                nc.scalar.activation(h2[:, 1, at], p2[1], ACT.Relu, bias=b2_sb[:, 1:2]).then_inc(h2_act, 1)

        @block.vector
        def _(dve):
            def copy(dst, src):
                return nc.vector.tensor_copy(dst, src)

            nc.vector.memset(w_pair[:, :, :], 0.0).then_inc(pair_zero, 1)
            for t in range(T):
                last = nc.vector.memset(xT[:, t, :, F:Q], 0.0)
            last.then_inc(pads_zero, 1)
            dve.wait_ge(wd_in, 32)
            nc.vector.tensor_tensor(w_dense[:, :], w_dense[:, :], w_dense2[:, :], ALU.add).then_inc(wd_ready, 1)
            for t in range(T):
                at = slice(t * P, (t + 1) * P)
                for k in range(GROUPS):
                    if (t * GROUPS + k) % 2 == 1:
                        collect(dve, copy, t, k, xt_dve)
                for m in range(CHUNKS):
                    regroup(dve, copy, t, m, (0, 1), z_dve)
                if t == 0:
                    dve.wait_ge(small_in, 64)
                dve.wait_ge(p1_ready, t + 1)
                for m in range(H1):
                    last = nc.vector.tensor_scalar(h1[:, m, at], p1[m], b1_sb[:, m:m + 1], 0.0, ALU.add, ALU.max)
                last.then_inc(h1_dve, 1)
                dve.wait_ge(p2_ready, t + 1)
                nc.vector.tensor_scalar(h2[:, 0, at], p2[0], b2_sb[:, 0:1], 0.0, ALU.add, ALU.max).then_inc(h2_dve, 1)
                dve.wait_ge(p3_ready, t + 1)
                nc.vector.tensor_copy(y[:, :, t], p3).then_inc(y_ready, 1)

        @block.tensor
        def _(pe):
            pe.wait_ge(ident_ready, 1)
            pe.wait_ge(dense_in, 16)
            pe.wait_ge(pads_zero, 1)

            def transposes(t, k):
                i = t * GROUPS + k
                tabled = sum(1 for f in group(k) if f >= 1)
                pe.wait_ge(gathered[t][k], 16 * tabled)
                if i >= 2:
                    pe.wait_ge(xt_dve if i % 2 else xt_act, i // 2)
                for n, f in enumerate(group(k)):
                    last = nc.tensor.transpose(turned[i % 2][:, n, :], rows[:, t, f, :], ident[:, :])
                last.then_inc(turned_ready, 1)

            def grams(t, m):
                n = t * CHUNKS + m
                if m == 0:
                    pe.wait_ge(xt_act, (GROUPS * (t + 1) + 1) // 2)
                    pe.wait_ge(xt_dve, GROUPS * (t + 1) // 2)
                if n >= 2:
                    pe.wait_ge(z_act, n - 1)
                    pe.wait_ge(z_dve, n - 1)
                for i in range(CHUNK):
                    at = PACK * (CHUNK * m + i)
                    four = xT[:, t, at:at + PACK, :]
                    last = nc.tensor.matmul(gram[n % 2][:, i, 0:PACK * F].rearrange("p (s g) -> p s g", s=PACK),
                                            four.rearrange("p s f -> p (s f)"), four[:, :, 0:F], start=True, stop=True)
                last.then_inc(gram_ready, 1)

            def layer1(t):
                if t == 0:
                    pe.wait_ge(wd_ready, 1)
                    pe.wait_ge(pair_in, 16 * n_pair)
                else:
                    pe.wait_ge(h1_act, t)
                    pe.wait_ge(h1_dve, t)
                dense_T = xT[:, t, :, 0]
                for m in range(M1):
                    nc.tensor.matmul(p1[m], w_dense[:, m:N1:M1], dense_T, start=(m % H1 == 0), stop=False,
                                     skip_group_check=True)
                pe.wait_ge(z_act, CHUNKS * (t + 1))
                pe.wait_ge(z_dve, CHUNKS * (t + 1))
                for c in range(ZC):
                    rows_c = Q * quads(c)
                    for m in range(M1):
                        last = nc.tensor.matmul(p1[m], w_pair[0:rows_c, c, m:N1:M1],
                                                z[0:rows_c, c, t * P:(t + 1) * P],
                                                start=False, stop=(c == ZC - 1), skip_group_check=True)
                last.then_inc(p1_ready, 1)

            def layers23(t):
                at = slice(t * P, (t + 1) * P)
                if t == 0:
                    pe.wait_ge(small_in, 64)
                pe.wait_ge(h1_act, t + 1)
                pe.wait_ge(h1_dve, t + 1)
                if t >= 1:
                    pe.wait_ge(y_ready, t)
                for m in range(M2):
                    for k in range(M1):
                        last = nc.tensor.matmul(p2[m], w2_sb[:, k, m:N2:M2], h1[:, k, at],
                                                start=(k == 0), stop=(k == M1 - 1))
                last.then_inc(p2_ready, 1)
                pe.wait_ge(h2_act, t + 1)
                pe.wait_ge(h2_dve, t + 1)
                for k in range(M2):
                    last = nc.tensor.matmul(p3, w3_sb[:, k:k + 1], h2[:, k, at], start=(k == 0), stop=(k == M2 - 1))
                last.then_inc(p3_ready, 1)

            for t in range(T):
                for k in range(GROUPS):
                    transposes(t, k)
                for m in range(CHUNKS):
                    grams(t, m)
                layer1(t)
                layers23(t)


_TABLES = [f"tbl_{i}" for i in range(26)]
_INS = ["r_dense_features", "ids", *_TABLES, "W_top1", "b_top1", "W_top2", "b_top2", "W_top3"]


def kernel(**inputs):
    import numpy as _np
    import concourse.bacc as _bacc
    from concourse import mybir as _mybir
    from concourse.bass_utils import run_bass_kernel_spmd as _run

    nc = _bacc.Bacc("TRN2", target_bir_lowering=False, num_devices=1)
    arrays, ap = {}, {}
    for name in _INS:
        a = _np.ascontiguousarray(inputs[name])
        arrays[f"in_{name}"] = a
        ap[name] = nc.dram_tensor(f"in_{name}", a.shape, _mybir.dt.from_np(a.dtype), kind="ExternalInput").ap()
    batch = inputs["ids"].shape[0]
    out = nc.dram_tensor("out_y", (batch, 1), _mybir.dt.float32, kind="ExternalOutput").ap()
    dlrm_tower(nc, ap["r_dense_features"], ap["ids"], [ap[n] for n in _TABLES], ap["W_top1"], ap["b_top1"],
               ap["W_top2"], ap["b_top2"], ap["W_top3"], out)
    r = _run(nc, [arrays], core_ids=[0])
    return r.results[0]["out_y"]
```

```python
from contextlib import ExitStack

import concourse.bass as bass
from concourse import mybir

F32 = mybir.dt.float32
F16 = mybir.dt.float16
BF16 = mybir.dt.bfloat16
I32 = mybir.dt.int32
ALU = mybir.AluOpType
ACT = mybir.ActivationFunctionType

P = 128
Q = 32
PACK = 4
TABBUF = 3
ROWBUF = 3
WARM = 9

LOOKED_UP = (2, 3, 5, 10, 11)
GROUPS = ((0, 4, 4), (1, 6, 3), (6, 3, 2), (14, 1, 3), (17, 1, 4), (21, 1, 4), (25, 1, 2))
ORDER = (("gram", 0), ("gram", 1), ("group", 0), ("gram", 2), ("group", 1), ("gram", 3), ("group", 2),
         ("dense", 0), ("pairs", 0), ("pairs", 1), ("group", 3), ("pairs", 2), ("pairs", 3), ("pairs", 4),
         ("group", 4), ("pairs", 5), ("pairs", 6), ("group", 5), ("layer", 2), ("group", 6), ("layer", 3))


def dlrm_tower(nc, dense, ids, ids_T, tables, w1, b1, w2, b2, w3, out):
    B, D = dense.shape
    NT = len(tables)
    F = NT + 1
    T = B // P
    N1, N2 = w2.shape
    M1, M2 = N1 // P, N2 // P
    PAIRS = F * (F - 1) // 2
    NG = len(GROUPS)
    ZC = -(-(F - 1) // 4)
    U = len(LOOKED_UP)
    V = tables[LOOKED_UP[0] - 1].shape[0]
    VC = 8
    VP = V // VC
    VBITS = 11
    features = [[a + s * i for i in range(n)] for a, s, n in GROUPS]
    fetched = [f for group in features for f in group if f >= 1]
    assert M1 == 4 and M2 == 2 and D == P and B == T * P and F <= Q and w1.shape[0] == 2 * D + PAIRS
    assert sorted(fetched + list(LOOKED_UP)) == list(range(1, F))
    assert V == VC * VP and VP <= P and V <= 2 ** VBITS
    assert all(tables[f - 1].shape[0] == V for f in LOOKED_UP)
    assert [k for what, k in ORDER if what == "pairs"] == list(range(ZC))
    assert [k for what, k in ORDER if what == "group"] == list(range(NG))

    STEPS = 4
    NQ = P // (PACK * STEPS)

    def quads(c):
        return min(4, F - 1 - 4 * c)

    ctx = ExitStack()
    with ctx:
        def sb(name, shape, dt=F32):
            return ctx.enter_context(nc.sbuf_tensor(name, shape, dt))

        def ps(name, shape):
            return ctx.enter_context(nc.psum_tensor(name, shape, F32))

        def sem(name):
            return ctx.enter_context(nc.semaphore(name))

        ids_sb = sb("ids_sb", [P, T, NT], I32)
        dense_rows = sb("dense_rows", [P, T, D])
        rows = sb("rows", [P, ROWBUF, len(fetched), D])
        ident = sb("ident", [P, P])
        xT = sb("xT", [P, T, P, Q])
        z = sb("z", [P, ZC, B])
        w_pair = sb("w_pair", [P, ZC, N1])
        w_dense = sb("w_dense", [P, N1])
        w_dense2 = sb("w_dense2", [P, N1])
        w2_sb = sb("w2_sb", [P, M1, N2])
        w3_sb = sb("w3_sb", [P, M2])
        b1_sb = sb("b1_sb", [P, M1])
        b2_sb = sb("b2_sb", [P, M2])
        h1 = sb("h1", [P, M1, P])
        h2 = sb("h2", [P, M2, P])
        y = sb("y", [1, P, T])
        warm = sb("warm", [P, 2])
        warm_pe = sb("warm_pe", [P, 4 * P], BF16)
        row_id = sb("row_id", [VP, VC])
        ids_all = [sb(f"ids_all{i}", [VP, B], I32) for i in range(2)]
        ids_16 = [sb(f"ids_16{i}", [VP, B], F16) for i in range(2)]
        onehot = [sb(f"onehot{i}", [VP, VC, B], BF16) for i in range(2)]
        table = [sb(f"table{i}", [VP, VC, D]) for i in range(TABBUF)]
        rest = [sb(f"rest{i}", [VP, VC, D]) for i in range(2)]
        low = [sb(f"low{i}", [VP, VC, D], BF16) for i in range(2)]

        turned = [ps(f"turned{i}", [P, 4, P]) for i in range(2)]
        gram = [ps(f"gram{i}", [P, NQ, P]) for i in range(2)]
        mlp = [ps(f"mlp{e}", [P, 2, 2 * P]) for e in range(2)]
        H1 = M1 // 2

        ids_in = sem("ids_in")
        dense_in = sem("dense_in")
        small_in = sem("small_in")
        wd_in = sem("wd_in")
        pair_in = sem("pair_in")
        ids_all_in = [sem(f"ids_all_in{u}") for u in range(U)]
        table_in = [sem(f"table_in{u}") for u in range(U)]
        gathered = [[sem(f"gathered{t}_{k}") for k in range(NG)] for t in range(T)]
        warm_in = sem("warm_in")
        warm_pe_in = sem("warm_pe_in")
        ident_zero = sem("ident_zero")
        ident_ready = sem("ident_ready")
        row_id_ready = sem("row_id_ready")
        pair_zero = sem("pair_zero")
        pads_zero = sem("pads_zero")
        wd_ready = sem("wd_ready")
        ids_16_ready = sem("ids_16_ready")
        onehot_ready = sem("onehot_ready")
        rest_ready = sem("rest_ready")
        low_ready = sem("low_ready")
        lookup_ready = sem("lookup_ready")
        lookup_out = sem("lookup_out")
        turned_ready = sem("turned_ready")
        xt_act = sem("xt_act")
        xt_dve = sem("xt_dve")
        gram_ready = sem("gram_ready")
        z_act = sem("z_act")
        z_dve = sem("z_dve")
        p1_ready = [sem(f"p1_ready{e}") for e in range(2)]
        h1_act = sem("h1_act")
        h1_dve = sem("h1_dve")
        p2_ready = [sem(f"p2_ready{e}") for e in range(2)]
        h2_act = sem("h2_act")
        h2_dve = sem("h2_dve")
        p3_ready = sem("p3_ready")
        y_ready = sem("y_ready")
        out_done = sem("out_done")
        block = ctx.enter_context(nc.Block())

        @block.sync
        def _(sp):
            sp.dma_start(ids_sb[:, :, :], ids.rearrange("(p t) f -> p t f", t=T)).then_inc(ids_in, 16)
            sp.dma_start(dense_rows[:, :, :], dense.rearrange("(p t) d -> p t d", t=T)).then_inc(dense_in, 16)
            sp.dma_start(w_dense[:, :], w1[0:D, :]).then_inc(wd_in, 16)
            sp.dma_start(w_dense2[:, :], w1[D + PAIRS:2 * D + PAIRS, :]).then_inc(wd_in, 16)
            sp.wait_ge(pair_zero, 1)
            for g in range(F - 1):
                c, j = divmod(g, 4)
                first = D + g * (F - 1) - g * (g - 1) // 2
                sp.dma_start(w_pair[Q * j + g + 1:Q * j + F, c, :], w1[first:first + F - 1 - g, :]).then_inc(pair_in, 16)
            sp.dma_start(b1_sb[:, :], b1.rearrange("(p m) -> p m", m=M1)).then_inc(small_in, 16)
            sp.dma_start(b2_sb[:, :], b2.rearrange("(p m) -> p m", m=M2)).then_inc(small_in, 16)
            sp.dma_start(w3_sb[:, :], w3.rearrange("(p m) o -> p (m o)", m=M2)).then_inc(small_in, 16)
            sp.dma_start(w2_sb[:, :, :], w2.rearrange("(p m) n -> p m n", m=M1)).then_inc(small_in, 16)
            sp.wait_ge(y_ready, T)
            sp.dma_start(out.rearrange("b o -> o b"), y[:, :, :].rearrange("o p t -> o (p t)")).then_inc(out_done, 16)
            sp.wait_ge(out_done, 16)

        @block.gpsimd
        def _(pool):
            pool.memset(warm[:, 0:1], 0.0).then_inc(warm_in, 1)
            pool.iota(row_id[:, :], [[1, VC]], base=0, channel_multiplier=VC,
                      allow_small_or_imprecise_dtypes=True).then_inc(row_id_ready, 1)
            pool.memset(ident[:, :], 0.0).then_inc(ident_zero, 1)
            pool.wait_ge(ident_zero, 1)
            pool.affine_select(out=ident[:, :], in_=ident[:, :], compare_op=ALU.not_equal, fill=1.0,
                               base=0, pattern=[[-1, P]], channel_multiplier=1).then_inc(ident_ready, 1)
            pool.wait_ge(ids_in, 16)
            for t in range(T):
                if t >= ROWBUF:
                    pool.wait_ge(turned_ready, NG * (t - ROWBUF + 1))
                for i, f in enumerate(fetched):
                    k = next(k for k in range(NG) if f in features[k])
                    pool.indirect_dma_start(
                        rows[:, t % ROWBUF, i, :], None, tables[f - 1],
                        bass.IndirectOffsetOnAxis(ap=ids_sb[:, t, f - 1:f], axis=0),
                    ).then_inc(gathered[t][k], 16)

        def groups_after_part(u, n):
            first = 3 * U - (NG - 1)
            k = 3 * u + n - first
            return [k] * (k >= 0) + [NG - 1] * (k == NG - 2)

        def collect(eng, copy, t, k, done):
            i = t * NG + k
            a, s, n = GROUPS[k]
            eng.wait_ge(turned_ready, i + 1)
            copy(xT[:, t, :, a:a + s * (n - 1) + 1:s],
                 turned[i % 2][:, 0:n, :].rearrange("p f b -> p b f")).then_inc(done, 1)

        def regroup(eng, copy, t, m, samples, done):
            n = t * STEPS + m
            eng.wait_ge(gram_ready, n + 1)
            for s in samples:
                for j in range(4):
                    cs = sum(1 for c in range(ZC) if quads(c) > j)
                    at = (F - 1) * s + j
                    src = gram[n % 2][Q * s:Q * (s + 1), :, at:at + 4 * (cs - 1) + 1:4]
                    at = t * P + PACK * NQ * m + s
                    dst = z[Q * j:Q * (j + 1), 0:cs, at:at + PACK * (NQ - 1) + 1:PACK]
                    last = copy(dst, src.rearrange("p q c -> p c q"))
            last.then_inc(done, 1)

        @block.scalar
        def _(act):
            def copy(dst, src):
                return nc.scalar.activation(dst, src, ACT.Copy)

            def load_ids(u):
                f = LOOKED_UP[u]
                src = ids_T[f - 1:f, :]
                src = bass.AP(src.tensor, src.offset, [[0, VP], [1, B]])
                act.dma_start(ids_all[u % 2][:, :], src).then_inc(ids_all_in[u], 16)

            def load_table(u):
                src = tables[LOOKED_UP[u] - 1].rearrange("(p c) d -> p c d", c=VC)
                act.dma_start(table[u % TABBUF][:, :, :], src).then_inc(table_in[u], 16)

            def narrow_ids(u):
                act.wait_ge(ids_all_in[u], 16)
                if u >= 2:
                    act.wait_ge(onehot_ready, VC * (u - 1))
                copy(ids_16[u % 2][:, :], ids_all[u % 2][:, :]).then_inc(ids_16_ready, 1)

            load_ids(0)
            load_table(0)
            act.wait_ge(warm_in, 1)
            copy(warm[:, 1:2], warm[:, 0:1])
            load_ids(1)
            for u in range(1, TABBUF):
                load_table(u)
            for u in range(2):
                narrow_ids(u)
                if u + 2 < U:
                    act.wait_ge(ids_16_ready, u + 1)
                    load_ids(u + 2)
            for u in range(U):
                if u + 2 < U:
                    narrow_ids(u + 2)
                    if u + 4 < U:
                        act.wait_ge(ids_16_ready, u + 3)
                        load_ids(u + 4)
                for n in range(3):
                    if n == 2:
                        act.wait_ge(lookup_ready, u + 1)
                        if u + TABBUF < U:
                            load_table(u + TABBUF)
                        copy(xT[:, :, :, LOOKED_UP[u]].rearrange("d t p -> d p t"),
                             mlp[u % 2][:, :, :].rearrange("d a (p t) -> d (a p) t", t=T)).then_inc(lookup_out, 1)
                    for k in groups_after_part(u, n):
                        if k % 2 == 0:
                            collect(act, copy, 0, k, xt_act)

            for t in range(T):
                for what, k in ORDER:
                    if what == "gram":
                        regroup(act, copy, t, k, (2, 3), z_act)
                    elif what == "group" and t + 1 < T and ((t + 1) * NG + k) % 2 == 0:
                        collect(act, copy, t + 1, k, xt_act)
                    elif what == "pairs" and k == ZC - 1:
                        if t == 0:
                            act.wait_ge(small_in, 64)
                        act.wait_ge(p1_ready[1], t + 1)
                        for m in range(H1, M1):
                            last = nc.scalar.activation(h1[:, m, :], mlp[1][:, m - H1, 0:P], ACT.Relu,
                                                        bias=b1_sb[:, m:m + 1])
                        last.then_inc(h1_act, 1)
                    elif what == "layer" and k == 2:
                        act.wait_ge(p2_ready[1], t + 1)
                        nc.scalar.activation(h2[:, 1, :], mlp[1][:, 0, 0:P], ACT.Relu,
                                             bias=b2_sb[:, 1:2]).then_inc(h2_act, 1)

        @block.vector
        def _(dve):
            def copy(dst, src):
                return nc.vector.tensor_copy(dst, src)

            def make_onehot(u):
                dve.wait_ge(ids_16_ready, u + 1)
                if u >= 2:
                    dve.wait_ge(lookup_ready, u - 1)
                for c in range(VC):
                    nc.vector.tensor_scalar(onehot[u % 2][:, c, :], ids_16[u % 2][:, :], row_id[:, c:c + 1],
                                            None, ALU.is_equal).then_inc(onehot_ready, 1)

            def split_table(u):
                dve.wait_ge(table_in[u], 16)
                if u >= 2:
                    dve.wait_ge(lookup_ready, u - 1)
                a, r = table[u % TABBUF], rest[u % 2]
                nc.vector.tensor_tensor(r[:, :, :], a[:, :, :], upper(a), ALU.subtract).then_inc(rest_ready, 1)
                dve.wait_ge(rest_ready, u + 1)
                nc.vector.tensor_tensor(low[u % 2][:, :, :], r[:, :, :], upper(r), ALU.subtract).then_inc(low_ready, 1)

            nc.vector.memset(warm_pe[:, :], 0.0).then_inc(warm_pe_in, 1)
            nc.vector.memset(w_pair[:, :, :], 0.0).then_inc(pair_zero, 1)
            dve.wait_ge(row_id_ready, 1)
            for u in range(U):
                make_onehot(u)
                split_table(u)
            dve.wait_ge(wd_in, 32)
            nc.vector.tensor_tensor(w_dense[:, :], w_dense[:, :], w_dense2[:, :], ALU.add).then_inc(wd_ready, 1)
            for k in range(1, NG, 2):
                if k == NG - 2:
                    nc.vector.memset(xT[:, :, :, F:Q], 0.0).then_inc(pads_zero, 1)
                collect(dve, copy, 0, k, xt_dve)

            for t in range(T):
                for what, k in ORDER:
                    if what == "gram":
                        regroup(dve, copy, t, k, (0, 1), z_dve)
                    elif what == "group" and t + 1 < T and ((t + 1) * NG + k) % 2 == 1:
                        collect(dve, copy, t + 1, k, xt_dve)
                    elif what == "pairs" and k == ZC - 1:
                        if t == 0:
                            dve.wait_ge(small_in, 64)
                        dve.wait_ge(p1_ready[0], t + 1)
                        for m in range(H1):
                            last = nc.vector.tensor_scalar(h1[:, m, :], mlp[0][:, m, 0:P], b1_sb[:, m:m + 1], 0.0,
                                                           ALU.add, ALU.max)
                        last.then_inc(h1_dve, 1)
                    elif what == "layer" and k == 2:
                        dve.wait_ge(p2_ready[0], t + 1)
                        nc.vector.tensor_scalar(h2[:, 0, :], mlp[0][:, 0, 0:P], b2_sb[:, 0:1], 0.0,
                                                ALU.add, ALU.max).then_inc(h2_dve, 1)
                    elif what == "layer" and k == 3:
                        dve.wait_ge(p3_ready, t + 1)
                        nc.vector.tensor_copy(y[:, :, t], mlp[0][0:1, 1, 0:P]).then_inc(y_ready, 1)

        @block.tensor
        def _(pe):
            def lookup(u):
                pe.wait_ge(table_in[u], 16)
                if u >= 2:
                    pe.wait_ge(lookup_out, u - 1)
                parts = (upper(table[u % TABBUF]), upper(rest[u % 2]), low[u % 2][:, :, :])
                for n, part in enumerate(parts):
                    if n == 1:
                        pe.wait_ge(low_ready, u + 1)
                    for c in range(VC):
                        if n == 0:
                            pe.wait_ge(onehot_ready, VC * u + c + 1)
                        last = nc.tensor.matmul(mlp[u % 2][:, :, :].rearrange("p a b -> p (a b)"), part[:, c, :],
                                                onehot[u % 2][:, c, :], start=(n == 0 and c == 0),
                                                stop=(n == 2 and c == VC - 1))
                    if n == 2:
                        last.then_inc(lookup_ready, 1)
                    for k in groups_after_part(u, n):
                        transposes(0, k)

            def transposes(t, k):
                i = t * NG + k
                if i == 0:
                    pe.wait_ge(ident_ready, 1)
                    pe.wait_ge(dense_in, 16)
                pe.wait_ge(gathered[t][k], 16 * sum(1 for f in features[k] if f >= 1))
                if i >= 2:
                    pe.wait_ge(xt_dve if i % 2 else xt_act, i // 2)
                for n, f in enumerate(features[k]):
                    src = rows[:, t % ROWBUF, fetched.index(f), :] if f else dense_rows[:, t, :]
                    last = nc.tensor.transpose(turned[i % 2][:, n, :], src, ident[:, :])
                last.then_inc(turned_ready, 1)

            def grams(t, m):
                n = t * STEPS + m
                if n == 0:
                    pe.wait_ge(lookup_out, U)
                    pe.wait_ge(pads_zero, 1)
                if m == 0:
                    pe.wait_ge(xt_act, (NG * (t + 1) + 1) // 2)
                    pe.wait_ge(xt_dve, NG * (t + 1) // 2)
                if n >= 2:
                    pe.wait_ge(z_act, n - 1)
                    pe.wait_ge(z_dve, n - 1)
                for i in range(NQ):
                    at = PACK * (NQ * m + i)
                    four = xT[:, t, at:at + PACK, :]
                    last = nc.tensor.matmul(gram[n % 2][:, i, 0:PACK * (F - 1)].rearrange("p (s g) -> p s g", s=PACK),
                                            four.rearrange("p s f -> p (s f)"), four[:, :, 0:F - 1],
                                            start=True, stop=True)
                last.then_inc(gram_ready, 1)

            def layer1_dense(t):
                if t == 0:
                    pe.wait_ge(wd_ready, 1)
                else:
                    pe.wait_ge(y_ready, t)
                    pe.wait_ge(h2_act, t)
                for m in range(M1):
                    nc.tensor.matmul(mlp[m // H1][:, m % H1, 0:P], w_dense[:, m:N1:M1], xT[:, t, :, 0],
                                     start=(m % H1 == 0), stop=False, skip_group_check=True)

            def layer1_pairs(t, c):
                if c == 0:
                    if t == 0:
                        pe.wait_ge(pair_in, 16 * (F - 1))
                    pe.wait_ge(z_act, STEPS * (t + 1))
                    pe.wait_ge(z_dve, STEPS * (t + 1))
                rows_c = Q * quads(c)
                for m in range(M1):
                    last = nc.tensor.matmul(mlp[m // H1][:, m % H1, 0:P], w_pair[0:rows_c, c, m:N1:M1],
                                            z[0:rows_c, c, t * P:(t + 1) * P],
                                            start=False, stop=(c == ZC - 1), skip_group_check=True)
                    if c == ZC - 1 and m % H1 == H1 - 1:
                        last.then_inc(p1_ready[m // H1], 1)

            def layer2(t):
                if t == 0:
                    pe.wait_ge(small_in, 64)
                pe.wait_ge(h1_dve, t + 1)
                for m in range(M2):
                    for k in range(M1):
                        if m == 0 and k == H1:
                            pe.wait_ge(h1_act, t + 1)
                        last = nc.tensor.matmul(mlp[m][:, 0, 0:P], w2_sb[:, k, m:N2:M2], h1[:, k, :],
                                                start=(k == 0), stop=(k == M1 - 1))
                    last.then_inc(p2_ready[m], 1)

            def layer3(t):
                for k in range(M2):
                    pe.wait_ge(h2_act if k else h2_dve, t + 1)
                    last = nc.tensor.matmul(mlp[0][0:1, 1, 0:P], w3_sb[:, k:k + 1], h2[:, k, :],
                                            start=(k == 0), stop=(k == M2 - 1))
                last.then_inc(p3_ready, 1)

            pe.wait_ge(warm_pe_in, 1)
            for _ in range(WARM):
                nc.tensor.matmul(mlp[1][:, :, :].rearrange("p a b -> p (a b)"), warm_pe[:, 0:P], warm_pe[:, :],
                                 start=True, stop=True)
            for u in range(U):
                lookup(u)
            for t in range(T):
                for what, k in ORDER:
                    if what == "gram":
                        grams(t, k)
                    elif what == "dense":
                        layer1_dense(t)
                    elif what == "pairs":
                        layer1_pairs(t, k)
                    elif what == "layer":
                        (layer2 if k == 2 else layer3)(t)
                    elif t + 1 < T:
                        transposes(t + 1, k)


def upper(a):
    return a[:, :, :].bitcast(BF16).rearrange("p c (d h) -> p c d h", h=2)[:, :, :, 1]


_TABLES = [f"tbl_{i}" for i in range(26)]
_INS = ["r_dense_features", "ids", *_TABLES, "W_top1", "b_top1", "W_top2", "b_top2", "W_top3"]


def kernel(**inputs):
    import numpy as _np
    import concourse.bacc as _bacc
    from concourse import mybir as _mybir
    from concourse.bass_utils import run_bass_kernel_spmd as _run

    nc = _bacc.Bacc("TRN2", target_bir_lowering=False, num_devices=1)
    arrays, ap = {}, {}
    for name in _INS:
        a = _np.ascontiguousarray(inputs[name])
        arrays[f"in_{name}"] = a
        ap[name] = nc.dram_tensor(f"in_{name}", a.shape, _mybir.dt.from_np(a.dtype), kind="ExternalInput").ap()
    ids_T = _np.ascontiguousarray(_np.asarray(inputs["ids"]).T)
    arrays["in_ids_T"] = ids_T
    ap["ids_T"] = nc.dram_tensor("in_ids_T", ids_T.shape, _mybir.dt.from_np(ids_T.dtype), kind="ExternalInput").ap()
    batch = inputs["ids"].shape[0]
    out = nc.dram_tensor("out_y", (batch, 1), _mybir.dt.float32, kind="ExternalOutput").ap()
    dlrm_tower(nc, ap["r_dense_features"], ap["ids"], ap["ids_T"], [ap[n] for n in _TABLES], ap["W_top1"], ap["b_top1"],
               ap["W_top2"], ap["b_top2"], ap["W_top3"], out)
    r = _run(nc, [arrays], core_ids=[0])
    return r.results[0]["out_y"]
```

```python
from contextlib import ExitStack

import concourse.bass as bass
from concourse import mybir

F32 = mybir.dt.float32
F32R = mybir.dt.float32r
BF16 = mybir.dt.bfloat16
I32 = mybir.dt.int32
ALU = mybir.AluOpType
ACT = mybir.ActivationFunctionType

P = 128
Q = 32
PACK = 4
ACT_CHUNKS = 1
TABBUF = 4
ROWBUF = 3
WARM = 12

LOOKED_UP = (2, 5, 10, 11, 14, 24, 25)
GROUPS = ((0, 4, 3), (1, 6, 4), (3, 3, 4), (15, 1, 4), (20, 1, 4), (26, 1, 1))
BEGIN = (("gram", 0), ("late layer", 3), ("gram", 1), ("group", 0), ("gram", 2), ("group", 1), ("gram", 3), ("group", 2),
         ("dense", 0), ("pairs", 3), ("pairs", 0), ("group", 3))
END = (("last pairs", 0), ("group", 4), ("group", 5), ("last pairs", 1), ("layer", 2))
LAST_END = (("last pairs", 0), ("last pairs", 1), ("layer", 2), ("group", 4), ("group", 5), ("layer", 3))


def dlrm_tower(nc, dense, ids, ids_T, tables, w1, b1, w2, b2, w3, out):
    B, D = dense.shape
    NT = len(tables)
    F = NT + 1
    T = B // P
    N1, N2 = w2.shape
    M1, M2 = N1 // P, N2 // P
    PAIRS = F * (F - 1) // 2
    NG = len(GROUPS)
    BLOCKS = -(-F // 4)
    ZC = (BLOCKS + 1) // 2
    MOVED = BLOCKS - ZC
    U = len(LOOKED_UP)
    V = tables[LOOKED_UP[0] - 1].shape[0]
    VC = 8
    VP = V // VC
    features = [[a + s * i for i in range(n)] for a, s, n in GROUPS]
    fetched = [f for group in features for f in group if f >= 1]
    assert M1 == 4 and M2 == 2 and D == P and B == T * P and F <= Q and w1.shape[0] == 2 * D + PAIRS
    assert sorted(fetched + list(LOOKED_UP)) == list(range(1, F))
    assert V == VC * VP and VP <= P
    assert all(tables[f - 1].shape[0] == V for f in LOOKED_UP)
    assert BLOCKS == 7 and ZC == 4 and TABBUF == 4
    assert [k for what, k in BEGIN if what == "pairs"] == [ZC - 1, 0]
    assert all([k for what, k in BEGIN + end if what == "group"] == list(range(NG)) for end in (END, LAST_END))

    STEPS = 4
    NQ = P // (PACK * STEPS)

    def work(t):
        for what, k in BEGIN + (END if t < T - 2 else LAST_END):
            if what == "late layer":
                if 0 < t < T - 1:
                    yield "layer", t - 1, k
            elif what == "group":
                if t + 1 < T:
                    yield "group", t + 1, k
            else:
                yield what, t, k

    def slot(b, c):
        return c if c < ZC else c - MOVED if b < MOVED else c - ZC

    ctx = ExitStack()
    with ctx:
        def sb(name, shape, dt=F32):
            return ctx.enter_context(nc.sbuf_tensor(name, shape, dt))

        def ps(name, shape):
            return ctx.enter_context(nc.psum_tensor(name, shape, F32))

        def sem(name):
            return ctx.enter_context(nc.semaphore(name))

        ids_sb = sb("ids_sb", [P, T, NT], I32)
        dense_rows = sb("dense_rows", [P, T, D])
        rows = sb("rows", [P, ROWBUF, len(fetched), D])
        ident = sb("ident", [P, P])
        xT = sb("xT", [P, T, P, Q])
        z = sb("z", [P, 2, BLOCKS, P])
        low_rows = sb("low_rows", [P, MOVED])
        high_rows = sb("high_rows", [P, MOVED])
        ones = sb("ones", [P, MOVED])
        w_pair = sb("w_pair", [P, ZC, N1])
        w_dense = sb("w_dense", [P, N1])
        w_dense2 = sb("w_dense2", [P, N1])
        w2_sb = sb("w2_sb", [P, M1, N2])
        w3_sb = sb("w3_sb", [P, M2])
        b1_sb = sb("b1_sb", [P, M1])
        b2_sb = sb("b2_sb", [P, M2])
        h1 = sb("h1", [P, M1, P])
        h2 = sb("h2", [P, M2, P])
        y = sb("y", [1, P, T])
        zero = sb("zero", [P, 1])
        act_warm = sb("act_warm", [P, 1])
        wake = sb("wake", [P, 4 * P], BF16)
        row_id = sb("row_id", [VP, VC])
        minus_row_id = sb("minus_row_id", [VP, VC])
        distance = [sb(f"distance{i}", [VP, B]) for i in range(2)]
        ids_all = [sb(f"ids_all{u}", [VP, B], I32) for u in range(U)]
        onehot = [sb(f"onehot{i}", [VP, VC, B], F32R) for i in range(2)]
        table = [sb(f"table{i}", [VP, VC, D]) for i in range(TABBUF)]
        high = [sb(f"high{i}", [VP, VC, D], F32R) for i in range(2)]
        low = [sb(f"low{i}", [VP, VC, D], F32R) for i in range(2)]

        turned = [ps(f"turned{i}", [P, 4, P]) for i in range(2)]
        gram = [ps(f"gram{i}", [P, NQ, P]) for i in range(2)]
        mlp = [ps(f"mlp{e}", [P, 2, 2 * P]) for e in range(2)]
        H1 = M1 // 2

        ids_in = sem("ids_in")
        dense_in = sem("dense_in")
        small_in = sem("small_in")
        wd_in = sem("wd_in")
        pair_in = sem("pair_in")
        ids_all_in = [sem(f"ids_all_in{u}") for u in range(U)]
        table_in = [sem(f"table_in{u}") for u in range(U)]
        gathered = [[sem(f"gathered{t}_{k}") for k in range(NG)] for t in range(T)]
        zero_in = sem("zero_in")
        warm_in = sem("warm_in")
        ident_zero = sem("ident_zero")
        ident_ready = sem("ident_ready")
        row_id_ready = sem("row_id_ready")
        pair_zero = sem("pair_zero")
        pads_zero = sem("pads_zero")
        wd_ready = sem("wd_ready")
        onehot_ready = sem("onehot_ready")
        onehot_act = sem("onehot_act")
        distance_ready = sem("distance_ready")
        high_ready = sem("high_ready")
        low_ready = sem("low_ready")
        lookup_ready = sem("lookup_ready")
        lookup_out = sem("lookup_out")
        turned_ready = sem("turned_ready")
        xt_act = sem("xt_act")
        xt_dve = sem("xt_dve")
        gram_ready = sem("gram_ready")
        z_act = sem("z_act")
        z_dve = sem("z_dve")
        z_low_merged = sem("z_low_merged")
        z_merged = sem("z_merged")
        ones_ready = sem("ones_ready")
        masks_ready = sem("masks_ready")
        p1_ready = [sem(f"p1_ready{e}") for e in range(2)]
        h1_act = sem("h1_act")
        h1_dve = sem("h1_dve")
        p2_ready = [sem(f"p2_ready{e}") for e in range(2)]
        h2_act = sem("h2_act")
        h2_dve = sem("h2_dve")
        p3_ready = sem("p3_ready")
        y_ready = sem("y_ready")
        out_done = sem("out_done")
        block = ctx.enter_context(nc.Block())

        def pair_row(a, b):
            return D + a * (F - 1) - a * (a - 1) // 2 + b - a - 1

        pair_loads = F - 1 + sum(BLOCKS - ZC - b for b in range(MOVED)) * 4

        @block.sync
        def _(sp):
            sp.dma_start(ids_sb[:, :, :], ids.rearrange("(p t) f -> p t f", t=T)).then_inc(ids_in, 16)
            sp.wait_ge(table_in[0], 16)
            sp.dma_start(dense_rows[:, :, :], dense.rearrange("(p t) d -> p t d", t=T)).then_inc(dense_in, 16)
            sp.dma_start(w_dense[:, :], w1[0:D, :]).then_inc(wd_in, 16)
            sp.dma_start(w_dense2[:, :], w1[D + PAIRS:2 * D + PAIRS, :]).then_inc(wd_in, 16)
            sp.wait_ge(table_in[2], 16)
            sp.wait_ge(pair_zero, 1)
            for g in range(F - 1):
                c, j = divmod(g, 4)
                n = min(4 * (c + ZC), F) - g - 1
                first = pair_row(g, g + 1)
                sp.dma_start(w_pair[Q * j + g + 1:Q * j + g + 1 + n, slot(c, c), :], w1[first:first + n, :])\
                    .then_inc(pair_in, 16)
            for f in range(4 * MOVED):
                b = f // 4
                for c, n in [(c, min(4, F - 4 * c)) for c in range(b + ZC, BLOCKS)]:
                    first = pair_row(f, 4 * c)
                    sp.dma_start(w_pair[f:f + Q * (n - 1) + 1:Q, slot(b, c), :], w1[first:first + n, :])\
                        .then_inc(pair_in, 16)
            sp.dma_start(b1_sb[:, :], b1.rearrange("(p m) -> p m", m=M1)).then_inc(small_in, 16)
            sp.dma_start(b2_sb[:, :], b2.rearrange("(p m) -> p m", m=M2)).then_inc(small_in, 16)
            sp.dma_start(w3_sb[:, :], w3.rearrange("(p m) o -> p (m o)", m=M2)).then_inc(small_in, 16)
            sp.dma_start(w2_sb[:, :, :], w2.rearrange("(p m) n -> p m n", m=M1)).then_inc(small_in, 16)
            sp.wait_ge(y_ready, T)
            sp.dma_start(out.rearrange("b o -> o b"), y[:, :, :].rearrange("o p t -> o (p t)")).then_inc(out_done, 16)
            sp.wait_ge(out_done, 16)

        @block.gpsimd
        def _(pool):
            pool.memset(zero[:, :], 0.0).then_inc(zero_in, 1)
            pool.iota(row_id[:, :], [[1, VC]], base=0, channel_multiplier=VC,
                      allow_small_or_imprecise_dtypes=True).then_inc(row_id_ready, 1)
            pool.iota(minus_row_id[:, :], [[-1, VC]], base=0, channel_multiplier=-VC,
                      allow_small_or_imprecise_dtypes=True).then_inc(row_id_ready, 1)
            pool.memset(ident[:, :], 0.0).then_inc(ident_zero, 1)
            pool.wait_ge(ident_zero, 1)
            pool.affine_select(out=ident[:, :], in_=ident[:, :], compare_op=ALU.not_equal, fill=1.0,
                               base=0, pattern=[[-1, P]], channel_multiplier=1).then_inc(ident_ready, 1)
            pool.memset(ones[:, :], 1.0).then_inc(ones_ready, 1)
            pool.wait_ge(ones_ready, 1)
            for j in range(4):
                rows_j = slice(Q * j, Q * (j + 1))
                pool.affine_select(out=low_rows[rows_j, :], in_=ones[rows_j, :], compare_op=ALU.is_gt, fill=0.0,
                                   base=4, pattern=[[4, MOVED]], channel_multiplier=-1).then_inc(masks_ready, 1)
                pool.affine_select(out=high_rows[rows_j, :], in_=ones[rows_j, :], compare_op=ALU.is_ge, fill=0.0,
                                   base=-4 * ZC, pattern=[[-4, MOVED]], channel_multiplier=1).then_inc(masks_ready, 1)
            pool.wait_ge(masks_ready, 8)
            pool.wait_ge(ids_in, 16)
            for t in range(T):
                if t >= ROWBUF:
                    pool.wait_ge(turned_ready, NG * (t - ROWBUF + 1))
                for i, f in enumerate(fetched):
                    k = next(k for k in range(NG) if f in features[k])
                    pool.indirect_dma_start(
                        rows[:, t % ROWBUF, i, :], None, tables[f - 1],
                        bass.IndirectOffsetOnAxis(ap=ids_sb[:, t, f - 1:f], axis=0),
                    ).then_inc(gathered[t][k], 16)

        def groups_after_part(u, n):
            k = 2 * (u + 1 - U) + n + NG - 1
            return [k] * (0 <= k < NG)

        def collect(eng, copy, t, k, done):
            i = t * NG + k
            a, s, n = GROUPS[k]
            eng.wait_ge(turned_ready, i + 1)
            copy(xT[:, t, :, a:a + s * (n - 1) + 1:s],
                 turned[i % 2][:, 0:n, :].rearrange("p f b -> p b f")).then_inc(done, 1)

        def regroup(eng, copy, t, m, samples, done):
            n = t * STEPS + m
            if t >= 2 and m == 0:
                eng.wait_ge(p1_ready[1], t - 1)
            eng.wait_ge(gram_ready, n + 1)
            for s in samples:
                for j in range(4):
                    at = 4 * BLOCKS * s + j
                    src = gram[n % 2][Q * s:Q * (s + 1), :, at:at + 4 * (BLOCKS - 1) + 1:4]
                    at = PACK * NQ * m + s
                    dst = z[Q * j:Q * (j + 1), t % 2, :, at:at + PACK * (NQ - 1) + 1:PACK]
                    last = copy(dst, src.rearrange("p q c -> p c q"))
            last.then_inc(done, 1)

        @block.scalar
        def _(act):
            def copy(dst, src):
                return nc.scalar.activation(dst, src, ACT.Copy)

            def load_ids(u):
                f = LOOKED_UP[u]
                src = ids_T[f - 1:f, :]
                src = bass.AP(src.tensor, src.offset, [[0, VP], [1, B]])
                act.dma_start(ids_all[u][:, :], src).then_inc(ids_all_in[u], 16)

            def load_table(u):
                src = tables[LOOKED_UP[u] - 1].rearrange("(p c) d -> p c d", c=VC)
                act.dma_start(table[u % TABBUF][:, :, :], src).then_inc(table_in[u], 16)

            def round_table(u):
                act.wait_ge(table_in[u], 16)
                if u >= 2:
                    act.wait_ge(lookup_ready, u - 1)
                copy(high[u % 2][:, :, :], table[u % TABBUF][:, :, :]).then_inc(high_ready, 1)

            def make_onehot(u):
                act.wait_ge(ids_all_in[u], 16)
                for c in range(VC - ACT_CHUNKS, VC):
                    n = ACT_CHUNKS * (u + 1) + c - VC
                    nc.scalar.activation(distance[n % 2][:, :], ids_all[u][:, :], ACT.Abs,
                                         bias=minus_row_id[:, c:c + 1]).then_inc(distance_ready, 1)
                    act.wait_ge(distance_ready, n + 1)
                    nc.scalar.activation(onehot[u % 2][:, c, :], distance[n % 2][:, :], ACT.Relu,
                                         bias=1.0, scale=-1.0).then_inc(onehot_act, 1)

            load_ids(0)
            load_table(0)
            act.wait_ge(zero_in, 1)
            copy(act_warm[:, :], zero[:, :])
            load_ids(1)
            load_table(1)
            act.wait_ge(row_id_ready, 2)
            for u in range(2):
                round_table(u)
                if u == 0:
                    load_ids(2)
                    load_table(2)
                make_onehot(u)
            load_ids(3)
            load_table(3)
            for u in range(U):
                if u == U - 1:
                    copy(xT[:, :, :, F:Q].rearrange("d t b f -> d (t b) f"),
                         zero[:, 0:1].rearrange("p (b f) -> p b f", f=1).broadcast_to([P, B, Q - F])).then_inc(pads_zero, 1)
                for n in range(2):
                    if n == 1:
                        if u + TABBUF < U:
                            act.wait_ge(high_ready, u + 1)
                            act.wait_ge(low_ready, u + 1)
                            load_ids(u + TABBUF)
                            load_table(u + TABBUF)
                        act.wait_ge(lookup_ready, u + 1)
                        if u + 2 < U:
                            round_table(u + 2)
                        found = mlp[u % 2][:, :, :].rearrange("d a (p t) -> d t (a p)", t=T)
                        if u == U - 1:
                            copy(xT[:, 0, :, LOOKED_UP[u]], found[:, 0, :]).then_inc(lookup_out, 1)
                            copy(xT[:, 1:T, :, LOOKED_UP[u]], found[:, 1:T, :]).then_inc(lookup_out, 1)
                        else:
                            copy(xT[:, :, :, LOOKED_UP[u]], found).then_inc(lookup_out, 1)
                        if u + 2 < U:
                            make_onehot(u + 2)
                    for k in groups_after_part(u, n):
                        if k % 2 == 0:
                            collect(act, copy, 0, k, xt_act)

            for what, t, k in [stage for tile in range(T) for stage in work(tile)]:
                if what == "gram":
                    regroup(act, copy, t, k, (2, 3), z_act)
                elif what == "group" and (t * NG + k) % 2 == 0:
                    collect(act, copy, t, k, xt_act)
                elif what == "last pairs" and k == 1:
                    if t == 0:
                        act.wait_ge(small_in, 64)
                    act.wait_ge(p1_ready[1], t + 1)
                    for m in range(H1, M1):
                        nc.scalar.activation(h1[:, m, :], mlp[1][:, m - H1, 0:P], ACT.Relu,
                                             bias=b1_sb[:, m:m + 1]).then_inc(h1_act, 1)
                elif what == "layer" and k == 2:
                    act.wait_ge(p2_ready[1], t + 1)
                    nc.scalar.activation(h2[:, 1, :], mlp[1][:, 0, 0:P], ACT.Relu,
                                         bias=b2_sb[:, 1:2]).then_inc(h2_act, 1)

        @block.vector
        def _(dve):
            def copy(dst, src):
                return nc.vector.tensor_copy(dst, src)

            def make_onehot(u):
                dve.wait_ge(ids_all_in[u], 16)
                if u >= 2:
                    dve.wait_ge(lookup_ready, u - 1)
                for c in range(VC - ACT_CHUNKS):
                    nc.vector.tensor_scalar(onehot[u % 2][:, c, :], ids_all[u][:, :], row_id[:, c:c + 1],
                                            None, ALU.is_equal).then_inc(onehot_ready, 1)

            def split_table(u):
                dve.wait_ge(high_ready, u + 1)
                if u >= 2:
                    dve.wait_ge(lookup_ready, u - 1)
                nc.vector.tensor_tensor(low[u % 2][:, :, :], table[u % TABBUF][:, :, :],
                                        high[u % 2][:, :, :].bitcast(F32), ALU.subtract).then_inc(low_ready, 1)

            def merge(t, m):
                n = t * STEPS + m
                samples = slice(PACK * NQ * m, PACK * NQ * (m + 1))
                moved = z[:, t % 2, ZC:BLOCKS, samples]
                dve.wait_ge(z_dve, n + 1)
                dve.wait_ge(z_act, n + 1)
                nc.vector.copy_predicated(z[:, t % 2, ZC - MOVED:ZC, samples], each(low_rows), moved)\
                    .then_inc(z_low_merged, 1)
                dve.wait_ge(z_low_merged, n + 1)
                nc.vector.copy_predicated(z[:, t % 2, 0:MOVED, samples], each(high_rows), moved).then_inc(z_merged, 1)

            def each(mask):
                return mask[:, :].bitcast(I32).rearrange("p (i o) -> p i o", o=1).broadcast_to([P, MOVED, PACK * NQ])

            nc.vector.memset(wake[:, :], 0.0).then_inc(warm_in, 1)
            nc.vector.memset(w_pair[:, :, :], 0.0).then_inc(pair_zero, 1)
            dve.wait_ge(row_id_ready, 1)
            for u in range(U):
                make_onehot(u)
                if u >= U - 2:
                    collect(dve, copy, 0, 2 * (u - U + 2) + 1, xt_dve)
                split_table(u)
            collect(dve, copy, 0, 5, xt_dve)
            dve.wait_ge(wd_in, 32)
            nc.vector.tensor_tensor(w_dense[:, :], w_dense[:, :], w_dense2[:, :], ALU.add).then_inc(wd_ready, 1)
            dve.wait_ge(masks_ready, 8)

            for what, t, k in [stage for tile in range(T) for stage in work(tile)]:
                if what == "gram":
                    regroup(dve, copy, t, k, (0, 1), z_dve)
                    merge(t, k)
                elif what == "group" and (t * NG + k) % 2 == 1:
                    collect(dve, copy, t, k, xt_dve)
                elif what == "last pairs" and k == 0:
                    if t == 0:
                        dve.wait_ge(small_in, 64)
                    dve.wait_ge(p1_ready[0], t + 1)
                    for m in range(H1):
                        last = nc.vector.tensor_scalar(h1[:, m, :], mlp[0][:, m, 0:P], b1_sb[:, m:m + 1], 0.0,
                                                       ALU.add, ALU.max)
                    last.then_inc(h1_dve, 1)
                elif what == "layer" and k == 2:
                    dve.wait_ge(p2_ready[0], t + 1)
                    nc.vector.tensor_scalar(h2[:, 0, :], mlp[0][:, 0, 0:P], b2_sb[:, 0:1], 0.0,
                                            ALU.add, ALU.max).then_inc(h2_dve, 1)
                elif what == "layer" and k == 3:
                    dve.wait_ge(p3_ready, t + 1)
                    nc.vector.tensor_copy(y[:, :, t], mlp[0][0:1, 1, 0:P]).then_inc(y_ready, 1)

        @block.tensor
        def _(pe):
            def lookup(u):
                pe.wait_ge(high_ready, u + 1)
                if u >= 2:
                    pe.wait_ge(lookup_out, u - 1)
                for n, part in enumerate((high[u % 2], low[u % 2])):
                    if n == 1:
                        pe.wait_ge(low_ready, u + 1)
                    for c in range(VC):
                        by_act = c - (VC - ACT_CHUNKS)
                        if n == 0 and by_act < 0:
                            pe.wait_ge(onehot_ready, (VC - ACT_CHUNKS) * u + c + 1)
                        elif n == 0:
                            pe.wait_ge(onehot_act, ACT_CHUNKS * u + by_act + 1)
                        last = nc.tensor.matmul(mlp[u % 2][:, :, :].rearrange("p a b -> p (a b)"), part[:, c, :],
                                                onehot[u % 2][:, c, :], start=(n == 0 and c == 0),
                                                stop=(n == 1 and c == VC - 1))
                    if n == 1:
                        last.then_inc(lookup_ready, 1)
                    for k in groups_after_part(u, n):
                        transposes(0, k)

            def transposes(t, k):
                i = t * NG + k
                if i == 0:
                    pe.wait_ge(ident_ready, 1)
                    pe.wait_ge(dense_in, 16)
                pe.wait_ge(gathered[t][k], 16 * sum(1 for f in features[k] if f >= 1))
                if i >= 2:
                    pe.wait_ge(xt_dve if i % 2 else xt_act, i // 2)
                for n, f in enumerate(features[k]):
                    src = rows[:, t % ROWBUF, fetched.index(f), :] if f else dense_rows[:, t, :]
                    last = nc.tensor.transpose(turned[i % 2][:, n, :], src, ident[:, :])
                last.then_inc(turned_ready, 1)

            def grams(t, m):
                n = t * STEPS + m
                if n == 0:
                    pe.wait_ge(lookup_out, U)
                    pe.wait_ge(pads_zero, 1)
                if n == STEPS:
                    pe.wait_ge(lookup_out, U + 1)
                if m == 0:
                    pe.wait_ge(xt_act, (NG * (t + 1) + 1) // 2)
                    pe.wait_ge(xt_dve, NG * (t + 1) // 2)
                if n >= 2:
                    pe.wait_ge(z_act, n - 1)
                    pe.wait_ge(z_dve, n - 1)
                for i in range(NQ):
                    at = PACK * (NQ * m + i)
                    four = xT[:, t, at:at + PACK, :]
                    last = nc.tensor.matmul(gram[n % 2][:, i, 0:PACK * 4 * BLOCKS].rearrange("p (s g) -> p s g", s=PACK),
                                            four.rearrange("p s f -> p (s f)"), four[:, :, 0:4 * BLOCKS],
                                            start=True, stop=True)
                last.then_inc(gram_ready, 1)

            def layer1_dense(t):
                if t == 0:
                    pe.wait_ge(wd_ready, 1)
                else:
                    pe.wait_ge(y_ready, t)
                    pe.wait_ge(h2_act, t)
                for m in range(M1):
                    nc.tensor.matmul(mlp[m // H1][:, m % H1, 0:P], w_dense[:, m:N1:M1], xT[:, t, :, 0],
                                     start=(m % H1 == 0), stop=False, skip_group_check=True)

            def layer1_chunk(t, c, units):
                for m in units:
                    last = nc.tensor.matmul(mlp[m // H1][:, m % H1, 0:P], w_pair[:, c, m:N1:M1],
                                            z[:, t % 2, c, :],
                                            start=False, stop=(c == ZC - 2), skip_group_check=True)
                return last

            def layer1_pairs(t, c):
                if t == 0 and c == ZC - 1:
                    pe.wait_ge(pair_in, 16 * pair_loads)
                if c == ZC - 1:
                    pe.wait_ge(z_low_merged, STEPS * (t + 1))
                else:
                    pe.wait_ge(z_merged, STEPS * (t + 1))
                layer1_chunk(t, c, range(M1))

            def layer1_last_pairs(t, e):
                for c in range(1, ZC - 1):
                    last = layer1_chunk(t, c, range(H1 * e, H1 * (e + 1)))
                last.then_inc(p1_ready[e], 1)

            def layer2(t):
                if t == 0:
                    pe.wait_ge(small_in, 64)
                pe.wait_ge(h1_dve, t + 1)
                for m in range(M2):
                    for k in range(M1):
                        if m == 0 and k >= H1:
                            pe.wait_ge(h1_act, H1 * t + k - H1 + 1)
                        last = nc.tensor.matmul(mlp[m][:, 0, 0:P], w2_sb[:, k, m:N2:M2], h1[:, k, :],
                                                start=(k == 0), stop=(k == M1 - 1))
                    last.then_inc(p2_ready[m], 1)

            def layer3(t):
                for k in range(M2):
                    pe.wait_ge(h2_act if k else h2_dve, t + 1)
                    last = nc.tensor.matmul(mlp[0][0:1, 1, 0:P], w3_sb[:, k:k + 1], h2[:, k, :],
                                            start=(k == 0), stop=(k == M2 - 1))
                last.then_inc(p3_ready, 1)

            pe.wait_ge(warm_in, 1)
            for _ in range(WARM):
                nc.tensor.matmul(mlp[1][:, :, :].rearrange("p a b -> p (a b)"), wake[:, 0:P], wake[:, :],
                                 start=True, stop=True)
            for u in range(U):
                lookup(u)
            for what, t, k in [stage for tile in range(T) for stage in work(tile)]:
                if what == "gram":
                    grams(t, k)
                elif what == "dense":
                    layer1_dense(t)
                elif what == "pairs":
                    layer1_pairs(t, k)
                elif what == "last pairs":
                    layer1_last_pairs(t, k)
                elif what == "layer":
                    (layer2 if k == 2 else layer3)(t)
                else:
                    transposes(t, k)


_TABLES = [f"tbl_{i}" for i in range(26)]
_INS = ["r_dense_features", "ids", *_TABLES, "W_top1", "b_top1", "W_top2", "b_top2", "W_top3"]


def kernel(**inputs):
    import numpy as _np
    import concourse.bacc as _bacc
    from concourse import mybir as _mybir
    from concourse.bass_utils import run_bass_kernel_spmd as _run

    nc = _bacc.Bacc("TRN2", target_bir_lowering=False, num_devices=1)
    arrays, ap = {}, {}
    for name in _INS:
        a = _np.ascontiguousarray(inputs[name])
        arrays[f"in_{name}"] = a
        ap[name] = nc.dram_tensor(f"in_{name}", a.shape, _mybir.dt.from_np(a.dtype), kind="ExternalInput").ap()
    ids_T = _np.ascontiguousarray(_np.asarray(inputs["ids"]).T)
    arrays["in_ids_T"] = ids_T
    ap["ids_T"] = nc.dram_tensor("in_ids_T", ids_T.shape, _mybir.dt.from_np(ids_T.dtype), kind="ExternalInput").ap()
    batch = inputs["ids"].shape[0]
    out = nc.dram_tensor("out_y", (batch, 1), _mybir.dt.float32, kind="ExternalOutput").ap()
    dlrm_tower(nc, ap["r_dense_features"], ap["ids"], ap["ids_T"], [ap[n] for n in _TABLES], ap["W_top1"], ap["b_top1"],
               ap["W_top2"], ap["b_top2"], ap["W_top3"], out)
    r = _run(nc, [arrays], core_ids=[0])
    return r.results[0]["out_y"]
```
